# Optimizing a Trainium2 kernel written in Bass

```python
import numpy as np
import jax
import jax.numpy as jnp

def _softmax(x, axis=-1):
    return jax.nn.softmax(x, axis=axis)

def _gelu(x):
    return jax.nn.gelu(x, approximate=True)

def _silu(x):
    return jax.nn.silu(x)

def _sigmoid(x):
    return jax.nn.sigmoid(x)

def _layernorm(x, axis=-1, eps=1e-05):
    m = jnp.mean(x, axis=axis, keepdims=True)
    v = jnp.var(x, axis=axis, keepdims=True)
    return (x - m) / jnp.sqrt(v + eps)

def _scatter_add(tgt, idx, src, axis=0):
    return tgt.at[idx].add(src)

def _segment_sum(src, seg, n):
    return jax.ops.segment_sum(src, seg, n)
kernel_name = 'mk_xattn_seq_d1_seqx_r4_582dd6'

def setup_inputs(seed: int=0):
    np.random.seed(seed)
    _w = jnp.asarray

    def _rec_inputs():
        import jax
        import jax.numpy as jnp
        _rk = jax.random.key(seed)
        x = -0.0003929 + 0.9999 * jax.random.normal(jax.random.fold_in(_rk, 1), (8, 256, 1024), jnp.float32)
        _lenS = 256 - jax.random.randint(jax.random.fold_in(_rk, 7), (8,), 0, max(1, 256 // 4) + 1, jnp.int32)
        _lenS2 = 256 - jax.random.randint(jax.random.fold_in(_rk, 8), (8,), 0, max(1, 256 // 4) + 1, jnp.int32)
        _ctx_4096P = jax.random.normal(jax.random.fold_in(_rk, 11), (8, 16, 1024), jnp.float32)
        _ctx_4096c = jax.random.dirichlet(jax.random.fold_in(_rk, 511), 0.3 * jnp.ones((16,), jnp.float32), (8, 256))
        _ctx_4096t = jnp.einsum('bsk,bkd->bsd', _ctx_4096c, _ctx_4096P)
        _ctx_4096t = _ctx_4096t * jax.lax.rsqrt(jnp.mean(jnp.square(_ctx_4096t)) + 1e-12) * 0.953939
        ctx_4096 = 2.81802e-05 + 1.00001 * (_ctx_4096t + 0.3 * jax.random.normal(jax.random.fold_in(_rk, 611), (8, 256, 1024), jnp.float32))
        return (x, ctx_4096)
    x, ctx_4096 = _rec_inputs()

    def _L0_xattn_setup():
        import jax, jax.numpy as jnp
        import numpy as np
        H = 1024
        NH = 32
        NKV = 8
        HD = H // NH
        R = 16
        SCALING = 32.0 / 16.0

        def _lora_linear(x, W, A, B):
            return x @ W + SCALING * (x @ A @ B)
        key = jax.random.key(seed)
        ks = jax.random.split(key, 16)
        d = {'hidden_states': jax.random.normal(ks[0], (4, 256, H), jnp.float32), 'traces': jax.random.normal(ks[1], (4, 256, H), jnp.float32), 'Wq': jax.random.normal(ks[2], (H, H), jnp.float32) * 0.02, 'Aq': jax.random.normal(ks[3], (H, R), jnp.float32) * 0.02, 'Bq': jax.random.normal(ks[4], (R, H), jnp.float32) * 0.02, 'Wk': jax.random.normal(ks[5], (H, NKV * HD), jnp.float32) * 0.02, 'Ak': jax.random.normal(ks[6], (H, R), jnp.float32) * 0.02, 'Bk': jax.random.normal(ks[7], (R, NKV * HD), jnp.float32) * 0.02, 'Wv': jax.random.normal(ks[8], (H, NKV * HD), jnp.float32) * 0.02, 'Av': jax.random.normal(ks[9], (H, R), jnp.float32) * 0.02, 'Bv': jax.random.normal(ks[10], (R, NKV * HD), jnp.float32) * 0.02, 'Wo': jax.random.normal(ks[11], (H, H), jnp.float32) * 0.02, 'Ao': jax.random.normal(ks[12], (H, R), jnp.float32) * 0.02, 'Bo': jax.random.normal(ks[13], (R, H), jnp.float32) * 0.02}
        return d
    _L0_xattn_all = _L0_xattn_setup()
    _L0_xattn_in = {k: v for k, v in _L0_xattn_all.items() if k in ('Wq', 'Aq', 'Bq', 'Wk', 'Ak', 'Bk', 'Wv', 'Av', 'Bv', 'Wo', 'Ao', 'Bo')}
    del _L0_xattn_all
    return {'x': x, 'ctx_4096': ctx_4096, 'L0_xattn_Wq': _L0_xattn_in['Wq'], 'L0_xattn_Aq': _L0_xattn_in['Aq'], 'L0_xattn_Bq': _L0_xattn_in['Bq'], 'L0_xattn_Wk': _L0_xattn_in['Wk'], 'L0_xattn_Ak': _L0_xattn_in['Ak'], 'L0_xattn_Bk': _L0_xattn_in['Bk'], 'L0_xattn_Wv': _L0_xattn_in['Wv'], 'L0_xattn_Av': _L0_xattn_in['Av'], 'L0_xattn_Bv': _L0_xattn_in['Bv'], 'L0_xattn_Wo': _L0_xattn_in['Wo'], 'L0_xattn_Ao': _L0_xattn_in['Ao'], 'L0_xattn_Bo': _L0_xattn_in['Bo']}

def reference(x, ctx_4096, L0_xattn_Wq, L0_xattn_Aq, L0_xattn_Bq, L0_xattn_Wk, L0_xattn_Ak, L0_xattn_Bk, L0_xattn_Wv, L0_xattn_Av, L0_xattn_Bv, L0_xattn_Wo, L0_xattn_Ao, L0_xattn_Bo):
    import jax
    import jax.numpy as jnp

    def _L0_xattn_ref(hidden_states, traces, Wq, Aq, Bq, Wk, Ak, Bk, Wv, Av, Bv, Wo, Ao, Bo):
        import jax, jax.numpy as jnp
        import numpy as np
        H = 1024
        NH = 32
        NKV = 8
        HD = H // NH
        R = 16
        SCALING = 32.0 / 16.0

        def _lora_linear(x, W, A, B):
            return x @ W + SCALING * (x @ A @ B)
        bsz, q_len, _ = hidden_states.shape
        t_len = traces.shape[1]
        groups = NH // NKV
        q = _lora_linear(hidden_states, Wq, Aq, Bq).reshape(bsz, q_len, NH, HD)
        q = jnp.transpose(q, (0, 2, 1, 3))
        k = _lora_linear(traces, Wk, Ak, Bk).reshape(bsz, t_len, NKV, HD)
        v = _lora_linear(traces, Wv, Av, Bv).reshape(bsz, t_len, NKV, HD)
        k = jnp.transpose(k, (0, 2, 1, 3))
        v = jnp.transpose(v, (0, 2, 1, 3))
        k = jnp.repeat(k, groups, axis=1)
        v = jnp.repeat(v, groups, axis=1)
        scores = jnp.einsum('bhqd,bhtd->bhqt', q, k) / jnp.sqrt(jnp.asarray(HD, q.dtype))
        attn = jax.nn.softmax(scores, axis=-1)
        context = jnp.einsum('bhqt,bhtd->bhqd', attn, v)
        context = jnp.transpose(context, (0, 2, 1, 3)).reshape(bsz, q_len, H)
        out = _lora_linear(context, Wo, Ao, Bo)
        return hidden_states + out
    x = _L0_xattn_ref(x, ctx_4096, L0_xattn_Wq, L0_xattn_Aq, L0_xattn_Bq, L0_xattn_Wk, L0_xattn_Ak, L0_xattn_Bk, L0_xattn_Wv, L0_xattn_Av, L0_xattn_Bv, L0_xattn_Wo, L0_xattn_Ao, L0_xattn_Bo)
    return x

_drawn_inputs = setup_inputs


def setup_inputs(seed=0):
    import zlib

    import numpy as np

    out = dict(_drawn_inputs(seed))
    spreads = {}
    factors = {'L0_xattn_Aq': 8.0, 'L0_xattn_Bq': 8.0, 'L0_xattn_Ak': 8.0, 'L0_xattn_Bk': 8.0}
    for name, (base, spread) in spreads.items():
        noise = np.random.default_rng([zlib.crc32(name.encode()), seed]).standard_normal(out[name].shape)
        drawn = base * np.exp(spread * noise) if base else spread * noise
        out[name] = jnp.asarray(drawn.astype(out[name].dtype))
    for name, factor in factors.items():
        out[name] = (out[name] * factor).astype(out[name].dtype)
    return out
```

```python
from contextlib import ExitStack

import concourse.bass as bass
from concourse import mybir

P = 128
NB = 8
S = 256
D = 1024
KT = D // P
HD = 32
NG = 8
GH = 4
KV = NG * HD
R = 4
LORA_SCALE = 2.0
SCORE_SCALE = float(HD) ** -0.5
SLOTS = 4 * NG
AHEAD = 4
FIRST = 3
GROUP_MM = 3 * KT
FILL = 9
DMA = 16

F32 = mybir.dt.float32
F32R = mybir.dt.float32r
ALU = mybir.AluOpType
ACT = mybir.ActivationFunctionType
AXIS = mybir.AxisListType.X

PROLOGUE = [("k", 0, 0), ("k", 1, 0), ("q", 0, 0), ("q", 1, 0), ("q", 2, 0), ("q", 3, 0),
            ("v", 0, 0), ("v", 1, 0)]
BODY = [("q", 4, 0), ("q", 5, 0), ("k", 0, 1), ("q", 6, 0), ("q", 7, 0), ("k", 1, 1),
        ("q", 0, 1), ("q", 1, 1), ("q", 2, 1), ("q", 3, 1), ("v", 0, 1), ("v", 1, 1)]
LAST = [g for g in BODY if g[2] == 0]
PRO = len(PROLOGUE)
PER = len(BODY)
SPLITS_PER = sum(g[0] != "v" for g in BODY)
SPLITS_PRO = sum(g[0] != "v" for g in PROLOGUE)
assert PER * GROUP_MM == SLOTS * FILL

FOLD_KV, FOLD_Q, FOLD_O = 0, KT, 3 * KT
FOLDS = 5 * KT


def xattn(nc, xt, ct, xn, wq, wkv, wo, a4, b4kv, b4q, b4o, out):
    with ExitStack() as ctx:
        def sb(name, shape, dt):
            return ctx.enter_context(nc.sbuf_tensor(name, shape, dt))

        def sem(name):
            return ctx.enter_context(nc.semaphore(name))

        w_hl = [sb("w_hi", [P, KT, D], F32R), sb("w_lo", [P, KT, D], F32R)]
        wkv_hl = [sb("wkv_hi", [P, KT, 2 * KV], F32R), sb("wkv_lo", [P, KT, 2 * KV], F32R)]
        x_hl = [sb("x_hi", [P, KT, S], F32R), sb("x_lo", [P, KT, S], F32R)]
        c_hl = [sb("c_hi", [P, KT, S], F32R), sb("c_lo", [P, KT, S], F32R)]
        raw = sb("raw", [P, 4, 2 * S], F32)
        q_stage = sb("q_stage", [P, 2, 2, S], F32R)
        k_stage = sb("k_stage", [P, 2, 2, S], F32R)
        q_stack = sb("q_stack", [P, 2, GH, S], F32R)
        k_stack = sb("k_stack", [P, NG, S], F32R)
        v_sb = sb("v_sb", [P, 2, KV], F32)
        probs = sb("probs", [P, 4, 2, S], F32)
        probs_t = sb("probs_t", [P, 2, 2, GH, S], F32)
        neg_max = sb("neg_max", [P, 4, 2], F32)
        sums = sb("sums", [P, 2, 2, GH], F32)
        rsums = sb("rsums", [P, 2, GH], F32)
        spread = sb("spread", [P, 2, 2, P], F32)
        rrow = sb("rrow", [P, S], F32)
        ctx_stage = sb("ctx_stage", [P, 2, S], F32)
        ident = sb("ident", [P, P], F32)
        lora = sb("lora", [P, 2, D], F32R)
        w_sum = sb("w_sum", [P, 2, 512], F32)

        probs_flat = probs[:].rearrange("p a b c -> p (a b c)")
        pt_flat = probs_t[:].rearrange("p a b c d -> p (a b c d)")
        lora_kv_a = q_stack[:].rearrange("p a b c -> p (a b c)")
        lora_kv_b = k_stack[:].rearrange("p a b -> p (a b)")
        w_raw = [pt_flat[:, 512 * i:512 * (i + 1)] for i in range(4)]
        w_raw_o = [raw[:, i, :] for i in range(4)]
        b_kv_raw = pt_flat[:, 3072:3584]
        ctx_raw = [pt_flat[:, 2048 * i:2048 * (i + 1)].rearrange("p (g n) -> p g n", g=NG)
                   for i in range(2)]
        o_parts = (c_hl, x_hl)
        x_rows = [probs_flat[:, D * i:D * (i + 1)] for i in range(2)]
        out_rows = [raw[:, 2 * i:2 * i + 2, :].rearrange("p a b -> p (a b)") for i in range(2)]

        banks = ctx.enter_context(nc.psum_tensor("banks", [P, 8, 512], F32))
        score_bank = [banks[:, i, :] for i in range(4)]
        turn_bank = [banks[:, 4 + i, :] for i in range(2)]
        proj_bank = [banks[:, 6 + i, :] for i in range(2)]

        q_dram = nc.dram_tensor("q_parts", [4, 2, P, S], F32, kind="Internal").ap()
        k_dram = nc.dram_tensor("k_parts", [2, 2, P, S], F32, kind="Internal").ap()
        ctx_dram = nc.dram_tensor("context", [NB, NG, P, S], F32, kind="Internal").ap()

        raw_in = [sem(f"raw_in{i}") for i in range(4)]
        w_in = [sem(f"w_in{i}") for i in range(4)]
        lora_in = [sem(f"lora_in{i}") for i in range(3)]
        q_stored = [sem(f"q_stored{i}") for i in range(2)]
        q_stacked = [sem(f"q_stacked{i}") for i in range(2)]
        k_stored = [sem(f"k_stored{i}") for i in range(2)]
        k_stacked = [sem(f"k_stacked{i}") for i in range(2)]
        ctx_stored = [sem(f"ctx_stored{i}") for i in range(2)]
        ctx_in = [sem(f"ctx_in{i}") for i in range(2)]
        rows_in = [sem(f"rows_in{i}") for i in range(2)]
        out_stored = [sem(f"out_stored{i}") for i in range(2)]
        sp_waits = sem("sp_waits")
        ident_zero = sem("ident_zero")
        ident_ready = sem("ident_ready")
        lora_hi = sem("lora_hi")
        lora_ready = sem("lora_ready")
        fold_mm = sem("fold_mm")
        w_summed = sem("w_summed")
        w_hi_done = sem("w_hi_done")
        w_lo_done = sem("w_lo_done")
        c_hi_done = sem("c_hi_done")
        c_ready = sem("c_ready")
        x_hi_done = sem("x_hi_done")
        x_ready = sem("x_ready")
        proj_mm = sem("proj_mm")
        proj_hi = sem("proj_hi")
        proj_out = sem("proj_out")
        scores_mm = sem("scores_mm")
        max_done = sem("max_done")
        exp_done = sem("exp_done")
        turned = sem("turned")
        pt_dve = sem("pt_dve")
        pt_act = sem("pt_act")
        rsum_done = sem("rsum_done")
        spread_done = sem("spread_done")
        ctx_mm = sem("ctx_mm")
        rrow_done = sem("rrow_done")
        ctx_done = sem("ctx_done")
        o_hi_done = sem("o_hi_done")
        o_ready = sem("o_ready")
        o_mm = sem("o_mm")
        o_out = sem("o_out")

        block = ctx.enter_context(nc.Block())

        def split_number(i, n):
            return n * SPLITS_PER + (SPLITS_PRO + sum(g[0] != "v" for g in BODY[:i]))

        def end_slot(i):
            return FIRST + (GROUP_MM * (i + 1) - 1) // FILL

        def chunk(s):
            return s // 4 % NG, s // 2 % 2, s % 2

        def fold_tile(f):
            return divmod(f - FOLD_Q, 2) if f < FOLD_O else ((f - FOLD_O) % KT, (f - FOLD_O) // KT)

        def w_raw_of(f):
            return (w_raw if f < FOLD_O else w_raw_o)[f % 4]

        def fold_bank(f):
            return score_bank[f % 3] if f < FOLD_O else proj_bank[f % 2]

        def w_piece(f, part):
            if f < FOLD_Q:
                return wkv_hl[part][:, f, :]
            kt, half = fold_tile(f)
            return w_hl[part][:, kt, 512 * half:512 * (half + 1)]

        def fold_chunks(s):
            early = (15, 16, 18, 19, 21, 22, 24, 25)
            if s in early:
                return [FOLD_O + early.index(s)]
            return [FOLD_O + KT + 2 * (s - 28) + i for i in range(2)] if 28 <= s < 32 else []

        def turn_of(unit, c):
            return turn_bank[(5 * unit + (0, 2, 3, 4)[c]) % 2]

        def copy_turned(op, unit, c):
            dst = probs_t[:, unit % 2, :, 2 * (c % 2):2 * (c % 2) + 2, P * (c // 2):P * (c // 2 + 1)]
            src = turn_of(unit, c).rearrange("p (t h q) -> p t h q", t=2, h=2)
            return op(dst, src, ACT.Copy) if op == nc.scalar.activation else op(dst, src)

        @block.sync
        def _(sp):
            def wait(semaphore, value):
                sp.wait_ge(semaphore, value)
                if not isinstance(value, int):
                    sp.sem_inc(sp_waits, 1)

            def load_inputs(src, b, j):
                sp.dma_start(raw[:, j, :], src[b, :, 2 * S * j:2 * S * (j + 1)]).then_inc(raw_in[j], DMA)

            def load_w(f):
                if f < FOLD_Q:
                    src = wkv[f]
                else:
                    kt, half = fold_tile(f)
                    src = (wq if f < FOLD_O else wo)[kt, :, 512 * half:512 * (half + 1)]
                if f >= 4:
                    wait(w_summed, f - 3)
                sp.dma_start(w_raw_of(f), src).then_inc(w_in[f % 4], DMA)

            def stack_q(g, fills_of_stage, scores_before):
                wait(q_stored[g % 2], fills_of_stage * DMA)
                if scores_before is not None:
                    wait(scores_mm, scores_before)
                for r, part in enumerate((0, 1, 0)):
                    sp.dma_start(q_stack[HD * r:HD * (r + 1), g % 2].bitcast(F32),
                                 q_dram[g % 4, part].rearrange("(c p) n -> p c n", c=GH)).then_inc(q_stacked[g % 2], DMA)

            def send_q(g, count):
                wait(proj_out, count)
                sp.dma_start(q_dram[g % 4].rearrange("h p n -> p h n"),
                             q_stage[:, g % 2].bitcast(F32)).then_inc(q_stored[g % 2], DMA)

            def send_k(m, count):
                wait(proj_out, count)
                sp.dma_start(k_dram[m].rearrange("h p n -> p h n"),
                             k_stage[:, m].bitcast(F32)).then_inc(k_stored[m], DMA)

            def stack_k(m, fills, scores_before):
                wait(k_stored[m], fills * DMA)
                if scores_before is not None:
                    wait(scores_mm, scores_before)
                for r, part in enumerate((0, 0, 1)):
                    sp.dma_start(k_stack[HD * r:HD * (r + 1), 4 * m:4 * m + 4].bitcast(F32),
                                 k_dram[m, part].rearrange("(c p) n -> p c n", c=4)).then_inc(k_stacked[m], DMA)

            for i in range(2):
                sp.dma_start(probs_flat[:, D * i:D * (i + 1)], a4[i]).then_inc(lora_in[0], DMA)
            sp.dma_start(b_kv_raw, b4kv).then_inc(lora_in[0], DMA)
            for f in range(4):
                load_w(f)
            for j in range(4):
                load_inputs(ct, 0, j)
            for f in range(4, FOLD_Q):
                load_w(f)
            wait(lora_ready, 1)
            sp.dma_start(probs_flat[:, 0:D], a4[2]).then_inc(lora_in[1], DMA)
            sp.dma_start(probs_flat[:, D:2 * D], b4q).then_inc(lora_in[1], DMA)
            for j in range(4):
                wait(c_ready, j + 1)
                load_inputs(xt, 0, j)
            for f in range(FOLD_Q, FOLD_Q + 4):
                load_w(f)
            wait(lora_ready, 2)
            sp.dma_start(probs_flat[:, 0:D], a4[3]).then_inc(lora_in[2], DMA)
            sp.dma_start(probs_flat[:, D:2 * D], b4o).then_inc(lora_in[2], DMA)
            wait(fold_mm, FOLD_Q)
            for m in range(2):
                send_k(m, m + 1)
                stack_k(m, 1, None)
            for f in range(FOLD_Q + 4, FOLD_O):
                load_w(f)
            for g in range(4):
                send_q(g, g + 3)
                if g < 2:
                    stack_q(g, 1, None)
            stack_q(2, 2, 4)
            for i in range(2):
                sp.sem_inc(ctx_stored[i], DMA)

            def body(b, last):
                late_w = iter(range(FOLD_O + 4, FOLDS))
                unit0 = b * NG
                group0 = b * PER + PRO
                score0 = b * SLOTS
                fills = b * 4

                def store_ctx(g):
                    wait(ctx_done, unit0 + (g + 1))
                    sp.dma_start(ctx_dram[b, g], ctx_stage[:, g % 2]).then_inc(ctx_stored[g % 2], DMA)

                def send(i):
                    kind, g, _ = BODY[i] if not last else LAST[i]
                    if kind == "q":
                        send_q(g, group0 + (i + 1))
                    else:
                        send_k(g, group0 + (i + 1))

                pos = {g: i for i, g in enumerate(LAST if last else BODY)}
                for j in range(4):
                    wait(x_ready, b * 4 + (j + 1))
                    if not last:
                        load_inputs(ct, b + 1, j)
                    else:
                        sp.dma_start(raw[:, j, :].rearrange("p (g n) -> p g n", g=2),
                                     ctx_dram[0, 2 * j:2 * j + 2].rearrange("g p n -> p g n")
                                     ).then_inc(raw_in[j], DMA)
                stack_q(3, fills + 2, score0 + 8)
                store_ctx(0)
                send(pos["q", 4, 0])
                stack_q(4, fills + 3, score0 + 12)
                send(pos["q", 5, 0])
                store_ctx(1)
                for j in range(4):
                    wait(c_ready, b * 4 + (j + 5))
                    if not last:
                        load_inputs(xt, b + 1, j)
                    else:
                        load_w(FOLD_O + j)
                stack_q(5, fills + 3, score0 + 16)
                if not last:
                    send(pos["k", 0, 1])
                    stack_k(0, b + 2, score0 + 16)
                store_ctx(2)
                send(pos["q", 6, 0])
                stack_q(6, fills + 4, score0 + 20)
                if last:
                    send(pos["q", 7, 0])
                    for g, loads in ((3, 2), (None, 2), (4, 1), (5, 3), (6, 2), (7, 2)):
                        for _ in range(loads):
                            load_w(next(late_w))
                        if g is None:
                            stack_q(7, fills + 4, score0 + 24)
                        else:
                            store_ctx(g)
                    return
                store_ctx(3)
                send(pos["q", 7, 0])
                stack_q(7, fills + 4, score0 + 24)
                send(pos["k", 1, 1])
                store_ctx(4)
                send(pos["q", 0, 1])
                stack_q(0, fills + 5, score0 + 28)
                store_ctx(5)
                send(pos["q", 1, 1])
                stack_q(1, fills + 5, score0 + 32)
                stack_k(1, b + 2, score0 + 32)
                send(pos["q", 2, 1])
                store_ctx(6)
                send(pos["q", 3, 1])
                stack_q(2, fills + 6, score0 + 36)
                store_ctx(7)

            with sp.Fori(0, NB - 1) as b:
                body(b, False)
            body(NB - 1, True)

            def load_ctx(v, i):
                sp.dma_start(ctx_raw[i], ctx_dram[v].rearrange("g p n -> p g n")).then_inc(ctx_in[i], DMA)

            def load_rows(v, h):
                sp.dma_start(x_rows[h], xn[v, P * h:P * (h + 1), :]).then_inc(rows_in[h], DMA)

            wait(turned, NB * SLOTS)
            for h in range(2):
                load_rows(0, h)
            wait(ctx_mm, NB * NG)
            for v in (1, 2):
                load_ctx(v, v % 2)
            for i in range(2):
                wait(ctx_stored[i], DMA * (1 + NB * NG // 2))

            def out_batch(v, i, more_ctx, more_rows):
                if more_ctx:
                    wait(o_ready, v + 1)
                    load_ctx(v + 3, 1 - i)
                for h in range(2):
                    wait(o_out, v * 4 + (2 * h + 2))
                    sp.dma_start(out[v, P * h:P * (h + 1), :], out_rows[h]).then_inc(out_stored[h], DMA)
                    if more_rows:
                        load_rows(v + 1, h)

            with sp.Fori(0, 2) as pair:
                for i in range(2):
                    out_batch(pair * 2 + i, i, True, True)
            for v in range(4, NB):
                out_batch(v, v % 2, v + 3 < NB, v + 1 < NB)
            for h in range(2):
                wait(out_stored[h], DMA * (NB + 1))

        @block.gpsimd
        def _(pool):
            nc.gpsimd.memset(ident[:], 0.0).then_inc(ident_zero, 1)
            pool.wait_ge(ident_zero, 1)
            nc.gpsimd.affine_select(out=ident[:], in_=ident[:], compare_op=ALU.not_equal, fill=1.0,
                                    base=0, pattern=[[-1, P]], channel_multiplier=1).then_inc(ident_ready, 1)

            def low(parts, j, hi_done, ready, count):
                cols = [t[:, 2 * j:2 * j + 2, :].rearrange("p a b -> p (a b)") for t in parts]
                pool.wait_ge(hi_done, count)
                nc.gpsimd.tensor_tensor(cols[1], raw[:, j, :], cols[0], ALU.subtract).then_inc(ready, 1)

            with pool.Fori(0, NB) as b:
                for j in range(4):
                    low(c_hl, j, c_hi_done, c_ready, b * 4 + (j + 1))
                for j in range(4):
                    low(x_hl, j, x_hi_done, x_ready, b * 4 + (j + 1))
            for j in range(4):
                low(c_hl, j, c_hi_done, c_ready, NB * 4 + (j + 1))
            for f in range(FOLD_O, FOLDS):
                pool.wait_ge(w_hi_done, f + 1)
                nc.gpsimd.tensor_tensor(w_piece(f, 1), w_sum[:, f % 2, :], w_piece(f, 0),
                                        ALU.subtract).then_inc(w_lo_done, 1)

        @block.scalar
        def _(act):
            def high(parts, j, done, fills):
                act.wait_ge(raw_in[j], fills * DMA)
                nc.scalar.activation(parts[0][:, 2 * j:2 * j + 2, :].rearrange("p a b -> p (a b)"),
                                     raw[:, j, :], ACT.Copy).then_inc(done, 1)

            def w_high(f):
                act.wait_ge(w_summed, f + 1)
                nc.scalar.activation(w_piece(f, 0), w_sum[:, f % 2, :], ACT.Copy).then_inc(w_hi_done, 1)

            def proj_high(kind, i, bank, group_id, stored):
                act.wait_ge(proj_mm, group_id + 1)
                if kind == "q":
                    if stored is not None:
                        act.wait_ge(q_stored[i % 2], stored)
                    nc.scalar.activation(q_stage[:, i % 2, 0, :], proj_bank[bank][:, 0:S],
                                         ACT.Copy).then_inc(proj_hi, 1)
                else:
                    if stored is not None:
                        act.wait_ge(k_stored[i], stored)
                    nc.scalar.activation(k_stage[:, i, 0, :], proj_bank[bank][:, 0:S],
                                         ACT.Copy, scale=-SCORE_SCALE).then_inc(proj_hi, 1)

            def exps(m, c):
                act.wait_ge(max_done, m + 1)
                for h in range(2):
                    last = nc.scalar.activation(
                        probs[:, c, h, :], score_bank[c][:, S * h:S * (h + 1)], ACT.Exp,
                        bias=neg_max[:, c, h:h + 1], scale=-1.0, accum_out=sum_at(m, c, h))
                last.then_inc(exp_done, 1)

            parity = [0]

            def sum_at(m, c, h):
                return sums[:, parity[0], c // 2, 2 * (c % 2) + h:2 * (c % 2) + h + 1]

            for j in range(4):
                high(c_hl, j, c_hi_done, 1)
            for f in range(FOLD_Q):
                w_high(f)
            for j in range(4):
                high(x_hl, j, x_hi_done, 2)
            for g in range(2):
                proj_high("k", g, g % 2, g, None)
            for f in range(FOLD_Q, FOLD_O):
                w_high(f)
            for g in range(4):
                proj_high("q", g, g % 2, 2 + g, DMA if g >= 2 else None)
            act.wait_ge(lora_ready, 3)
            for m in range(4):
                parity[0] = 0
                exps(m, m)

            def slot(b, s, last, prologue=False):
                n = b * SLOTS
                g, qh, hp = chunk(s)
                unit = s // 4
                c = s % 4
                if c == 3:
                    act.wait_ge(turned, n + (s + 1))
                    copy_turned(nc.scalar.activation, unit, c).then_inc(pt_act, 1)
                if not prologue and c == 1 and s >= 5:
                    act.wait_ge(ctx_mm, b * NG + unit)
                    nc.scalar.activation(rrow[:], turn_bank[(5 * unit + 1) % 2][:, S:2 * S],
                                         ACT.Copy).then_inc(rrow_done, 1)
                groups = [] if prologue else (LAST if last else BODY)
                for i, (kind, gi, nxt) in enumerate(groups):
                    if end_slot(i) + 1 == s and kind != "v":
                        fills = b * 4 + (4 * nxt + gi // 2) if kind == "q" else b + 1
                        proj_high(kind, gi, i % 2, b * PER + (PRO + i), fills * DMA)
                if not (last and s + AHEAD >= SLOTS):
                    parity[0] = (unit + 1) % 2
                    act.wait_ge(turned, n + (s + 1))
                    if c == 0 and not (prologue and s == 0):
                        act.wait_ge(rsum_done, b * NG + unit)
                    exps(n + (s + AHEAD), c)
                if last:
                    for f in fold_chunks(s):
                        w_high(f)
                if not prologue and s in (5, 6):
                    for j in (2 * (s - 5), 2 * (s - 5) + 1):
                        act.wait_ge(proj_mm, b * PER + PRO)
                        high(c_hl, j, c_hi_done, b * 2 + 3)
                if not prologue and not last and s in (16, 17):
                    for j in (2 * (s - 16), 2 * (s - 16) + 1):
                        act.wait_ge(proj_mm, b * PER + (PRO + BODY.index(("q", 7, 0)) + 1))
                        high(x_hl, j, x_hi_done, b * 2 + 4)

            for s in range(FIRST):
                slot(0, s, False, True)
            with act.Fori(0, NB - 1) as b:
                for s in range(FIRST, FIRST + SLOTS):
                    slot(b, s, False)
            for s in range(FIRST, SLOTS + 2):
                slot(NB - 1, s, True)

            def o_high(i, fills):
                act.wait_ge(ctx_in[i], fills * DMA)
                nc.scalar.activation(o_parts[i][0][:], ctx_raw[i], ACT.Copy).then_inc(o_hi_done, 1)

            o_high(1, 1)
            with act.Fori(1, NB // 2) as pair:
                for i in range(2):
                    act.wait_ge(o_mm, pair * 8 + (4 * i - 4))
                    o_high(i, pair + i)

        @block.vector
        def _(dve):
            def build_stack(a_raw, b_raw, a_dst, b_dst, fold, n, count):
                dve.wait_ge(lora_in[n], DMA * count)
                if fold:
                    dve.wait_ge(fold_mm, fold)
                nc.vector.tensor_copy(a_dst, a_raw)
                nc.vector.tensor_copy(b_dst, b_raw).then_inc(lora_hi, 1)
                dve.wait_ge(lora_hi, n + 1)
                nc.vector.tensor_tensor(a_dst[64:128], a_raw[64:128], a_dst[64:128], ALU.subtract)
                nc.vector.tensor_tensor(b_dst[32:64], b_raw[32:64], b_dst[32:64], ALU.subtract)
                nc.vector.tensor_tensor(b_dst[96:128], b_raw[96:128], b_dst[96:128],
                                        ALU.subtract).then_inc(lora_ready, 1)

            def w_total(f):
                dve.wait_ge(fold_mm, f + 1)
                dve.wait_ge(w_in[f % 4], DMA * (f // 4 + 1))
                if f >= 2:
                    dve.wait_ge(w_lo_done, f - 1)
                nc.vector.scalar_tensor_tensor(
                    out=w_sum[:, f % 2, :], in0=fold_bank(f), scalar=LORA_SCALE, in1=w_raw_of(f),
                    op0=ALU.mult, op1=ALU.add).then_inc(w_summed, 1)

            def w_low(f):
                dve.wait_ge(w_hi_done, f + 1)
                nc.vector.tensor_tensor(w_piece(f, 1), w_sum[:, f % 2, :], w_piece(f, 0),
                                        ALU.subtract).then_inc(w_lo_done, 1)

            def fold(f0, f1):
                for f in range(f0, f1):
                    w_total(f)
                    if f > f0:
                        w_low(f - 1)
                w_low(f1 - 1)

            def proj_low(kind, i, bank, group_id, splits, ctxs):
                src = proj_bank[bank][:, 0:S]
                if kind == "v":
                    dve.wait_ge(proj_mm, group_id + 1)
                    if ctxs is not None:
                        dve.wait_ge(ctx_mm, ctxs)
                    nc.vector.tensor_copy(v_sb[:, i, :], src).then_inc(proj_out, 1)
                elif kind == "k":
                    dve.wait_ge(proj_hi, splits)
                    nc.vector.scalar_tensor_tensor(
                        out=k_stage[:, i, 1, :], in0=src, scalar=-SCORE_SCALE, in1=k_stage[:, i, 0, :],
                        op0=ALU.mult, op1=ALU.subtract).then_inc(proj_out, 1)
                else:
                    dve.wait_ge(proj_hi, splits)
                    nc.vector.tensor_tensor(q_stage[:, i % 2, 1, :], src, q_stage[:, i % 2, 0, :],
                                            ALU.subtract).then_inc(proj_out, 1)

            def row_max(m, c):
                dve.wait_ge(scores_mm, m + 1)
                nc.vector.tensor_reduce(out=neg_max[:, c, :],
                                        in_=score_bank[c].rearrange("p (h t) -> p h t", h=2),
                                        axis=AXIS, op=ALU.min).then_inc(max_done, 1)

            build_stack(probs_flat[:, 0:2 * D], b_kv_raw, lora_kv_a[:, 0:2 * D], lora_kv_b[:, 0:2 * KV],
                        0, 0, 3)
            fold(FOLD_KV, FOLD_Q)
            for n, f in ((1, 0), (2, FOLD_O)):
                if n == 2:
                    fold(FOLD_Q, FOLD_O)
                build_stack(probs_flat[:, 0:D], probs_flat[:, D:2 * D], lora[:, 0, :], lora[:, 1, :],
                            f, n, 2)
                if n == 1:
                    for m in range(2):
                        proj_low("k", m, m % 2, m, m + 1, None)
            for g in range(4):
                proj_low("q", g, g % 2, 2 + g, 3 + g, None)
            proj_low("v", 0, 0, 6, None, None)
            for m in range(4):
                row_max(m, m)

            def slot(b, s, last, prologue=False):
                n = b * SLOTS
                unit, c = s // 4, s % 4
                if c == 1 and not prologue:
                    u = unit - 1
                    dve.wait_ge(rrow_done, b * NG + (u + 1))
                    dve.wait_ge(ctx_stored[u % 2], b * (4 * DMA) + DMA * (u // 2 + 1))
                    nc.vector.tensor_tensor(ctx_stage[:, u % 2, :], turn_bank[(5 * unit + 1) % 2][:, 0:S],
                                            rrow[:], ALU.mult).then_inc(ctx_done, 1)
                if c != 3 and not (last and s >= SLOTS):
                    dve.wait_ge(turned, n + (s + 1))
                    copy_turned(nc.vector.tensor_copy, unit, c).then_inc(pt_dve, 1)
                if not (last and s + AHEAD >= SLOTS):
                    row_max(n + (s + AHEAD), c)
                if prologue:
                    return
                if c == 3:
                    dve.wait_ge(exp_done, n + (s + 1))
                    nc.vector.reciprocal(rsums[:], sums[:, unit % 2]).then_inc(rsum_done, 1)
                    dve.wait_ge(rsum_done, b * NG + (unit + 1))
                    for qh in range(2):
                        last_op = nc.vector.tensor_copy(
                            spread[:, unit % 2, qh].rearrange("p (h d) -> p h d", h=GH),
                            rsums[:, qh, :].unsqueeze(2).broadcast_to([P, GH, HD]))
                    last_op.then_inc(spread_done, 1)
                if s == FIRST:
                    proj_low("v", 1, 1, b * PER + (PRO - 1), None, None)
                if last:
                    for f in fold_chunks(s):
                        w_total(f)
                for i, (kind, gi, nxt) in enumerate(LAST if last else BODY):
                    if end_slot(i) + 1 == s:
                        proj_low(kind, gi, i % 2, b * PER + (PRO + i),
                                 split_number(i + 1, b) if kind != "v" and not last else
                                 b * SPLITS_PER + (SPLITS_PRO + i + 1),
                                 b * NG + NG)

            for s in range(FIRST):
                slot(0, s, False, True)
            with dve.Fori(0, NB - 1) as b:
                for s in range(FIRST, FIRST + SLOTS):
                    slot(b, s, False)
            for s in range(FIRST, SLOTS + 2):
                slot(NB - 1, s, True)

            for h in range(2):
                dve.sem_inc(out_stored[h], DMA)

            def o_low(i, count):
                dve.wait_ge(o_hi_done, count)
                nc.vector.tensor_tensor(o_parts[i][1][:], ctx_raw[i], o_parts[i][0][:],
                                        ALU.subtract).then_inc(o_ready, 1)

            def rows_out(v, i):
                for h in range(2):
                    dve.wait_ge(rows_in[h], v * DMA + DMA)
                    dve.wait_ge(out_stored[h], v * DMA + DMA)
                    for half in range(2):
                        dve.wait_ge(o_mm, v * 4 + ((1, 3), (3, 4))[h][half])
                        cols = slice(512 * half, 512 * (half + 1))
                        nc.vector.tensor_tensor(out_rows[h][:, cols], banks[:, 4 * i + 2 * h + half, :],
                                                x_rows[h][:, cols], ALU.add).then_inc(o_out, 1)

            with dve.Fori(0, NB // 2 - 1) as pair:
                for i in range(2):
                    o_low(1 - i, pair * 2 + (i + 1))
                    rows_out(pair * 2 + i, i)
            o_low(1, NB - 1)
            rows_out(NB - 2, 0)
            rows_out(NB - 1, 1)

        @block.tensor
        def _(pe):
            def fold_mms(f):
                if f >= 3:
                    pe.wait_ge(w_summed, f - 2 if f < FOLD_O else f - 1)
                bank = fold_bank(f)
                if f < FOLD_Q:
                    for i in range(2):
                        last = nc.tensor.matmul(bank[:, KV * i:KV * (i + 1)],
                                                lora_kv_a[:, D * i + P * f:D * i + P * (f + 1)],
                                                lora_kv_b[:, KV * i:KV * (i + 1)], start=True, stop=True)
                else:
                    kt, half = fold_tile(f)
                    last = nc.tensor.matmul(bank, lora[:, 0, P * kt:P * (kt + 1)],
                                            lora[:, 1, 512 * half:512 * (half + 1)], start=True, stop=True)
                last.then_inc(fold_mm, 1)

            def group_step(kind, i, bank, k):
                kt, product = divmod(k, 3)
                w_part, t_part = ((0, 0), (0, 1), (1, 0))[product]
                if kind == "q":
                    lhs, rhs = w_hl[w_part][:, kt, P * i:P * (i + 1)], x_hl[t_part][:, kt, :]
                elif kind == "k":
                    lhs, rhs = wkv_hl[w_part][:, kt, P * i:P * (i + 1)], c_hl[t_part][:, kt, :]
                else:
                    lhs, rhs = c_hl[t_part][:, kt, P * i:P * (i + 1)], wkv_hl[w_part][:, kt, KV:2 * KV]
                mm = nc.tensor.matmul(proj_bank[bank][:, 0:S], lhs, rhs, start=(k == 0),
                                      stop=(k == GROUP_MM - 1))
                if k == GROUP_MM - 1:
                    mm.then_inc(proj_mm, 1)

            def inputs_ready(kind, i, k, batches):
                if i == 0 and kind in "qk" and k % 6 == 0:
                    pe.wait_ge(x_ready if kind == "q" else c_ready, batches * 4 + (k // 6 + 1))

            def scores(m, g, c):
                qh, hp = c // 2, c % 2
                for h in range(2):
                    head = 2 * hp + h
                    last = nc.tensor.matmul(
                        score_bank[c][:, S * h:S * (h + 1)],
                        q_stack[0:3 * HD, g % 2, head, P * qh:P * (qh + 1)],
                        k_stack[0:3 * HD, g, :], start=True, stop=True)
                last.then_inc(scores_mm, 1)

            def stacks_ready(b, g):
                pe.wait_ge(q_stacked[g % 2], b * (12 * DMA) + 3 * DMA * (g // 2 + 1))
                if g % 4 == 0:
                    pe.wait_ge(k_stacked[g // 4], b * (3 * DMA) + 3 * DMA)

            def turn(unit, c):
                bank = turn_of(unit, c)
                for t in range(2):
                    for h in range(2):
                        last = nc.tensor.transpose(bank[:, P * (2 * t + h):P * (2 * t + h + 1)],
                                                   probs[:, c, h, P * t:P * (t + 1)], ident[:])
                last.then_inc(turned, 1)

            def context(unit):
                bank = turn_bank[(5 * unit + 6) % 2]
                for qh in range(2):
                    nc.tensor.transpose(bank[:, S + P * qh:S + P * (qh + 1)], spread[:, unit % 2, qh],
                                        ident[:])
                for t in range(2):
                    for h in range(GH):
                        last = nc.tensor.matmul(
                            bank[HD * h:HD * (h + 1), 0:S],
                            v_sb[:, t, HD * (unit % NG):HD * (unit % NG + 1)],
                            probs_t[:, unit % 2, t, h, :], start=(t == 0), stop=(t == 1),
                            tile_position=(0, HD * h))
                last.then_inc(ctx_mm, 1)

            def out_step(i, qh, half, k):
                kt, product = divmod(k, 3)
                w_part, t_part = ((0, 0), (0, 1), (1, 0))[product]
                mm = nc.tensor.matmul(
                    banks[:, 4 * i + 2 * qh + half, :], o_parts[i][t_part][:, kt, P * qh:P * (qh + 1)],
                    w_hl[w_part][:, kt, 512 * half:512 * (half + 1)],
                    start=(k == 0), stop=(k == GROUP_MM - 1))
                if k == GROUP_MM - 1:
                    mm.then_inc(o_mm, 1)

            pe.wait_ge(lora_ready, 1)
            for f in range(FOLD_Q):
                fold_mms(f)
            for j, (kind, i, _) in enumerate(PROLOGUE):
                if j == 2:
                    pe.wait_ge(lora_ready, 2)
                    for f in range(FOLD_Q, FOLD_O):
                        fold_mms(f)
                if j >= 2:
                    pe.wait_ge(proj_out, j - 1)
                for k in range(GROUP_MM):
                    inputs_ready(kind, i, k, 0)
                    if j == 0 and k % 3 == 0:
                        pe.wait_ge(w_lo_done, k // 3 + 1)
                    if j == 2 and k % 3 == 0:
                        pe.wait_ge(w_lo_done, FOLD_Q + 2 * (k // 3) + 2)
                    group_step(kind, i, j % 2, k)
            pe.wait_ge(ident_ready, 1)
            for m in range(4):
                if m == 0:
                    stacks_ready(0, 0)
                scores(m, 0, m)

            def slot(b, s, last, prologue=False):
                n = b * SLOTS
                unit, c = s // 4, s % 4
                if s < SLOTS or not last:
                    pe.wait_ge(exp_done, n + (s + 1))
                    if c == 0 and not prologue:
                        pe.wait_ge(pt_dve, b * (3 * NG) + 3 * unit)
                    if c in (1, 3):
                        pe.wait_ge(pt_dve, b * (3 * NG) + (3 * unit + (c + 1) // 2))
                    if c == 2 and not prologue:
                        pe.wait_ge(ctx_done, b * NG + unit)
                    turn(unit, c)
                if not (last and s + AHEAD >= SLOTS):
                    nxt = (s + AHEAD) // 4
                    if c == 0:
                        if nxt < NG:
                            stacks_ready(b, nxt)
                        else:
                            stacks_ready(b + 1, nxt % NG)
                    scores(n + (s + AHEAD), nxt % NG, c)
                if prologue:
                    return
                groups = LAST if last else BODY
                for k in range(FILL * (s - FIRST), FILL * (s - FIRST + 1)):
                    j, step = divmod(k, GROUP_MM)
                    if j >= len(groups):
                        break
                    kind, i, nx = groups[j]
                    if step == 0:
                        pe.wait_ge(proj_out, b * PER + (PRO + j - 1))
                    if nx:
                        inputs_ready(kind, i, step, b + 1)
                    group_step(kind, i, j % 2, step)
                if c == 0:
                    u = unit - 1
                    pe.wait_ge(pt_act, b * NG + (u + 1))
                    pe.wait_ge(pt_dve, b * (3 * NG) + 3 * (u + 1))
                    pe.wait_ge(spread_done, b * NG + (u + 1))
                    if u == 0:
                        pe.wait_ge(proj_out, b * PER + PRO)
                    context(u)
                if last:
                    chunks = fold_chunks(s)
                    if s < 28:
                        for f in chunks:
                            if f == FOLD_O:
                                pe.wait_ge(proj_out, b * PER + (PRO + len(LAST)))
                            fold_mms(f)
                    elif s < SLOTS:
                        qh = (s - 28) // 2
                        if s == 28:
                            pe.wait_ge(c_ready, 4 * NB + 4)
                            pe.wait_ge(w_lo_done, FOLD_O + KT)
                        if s == 30:
                            pe.wait_ge(exp_done, n + 31)
                        for k in range(GROUP_MM // 2):
                            if k % 6 == 0:
                                fold_mms(chunks[k // 6])
                            out_step(0, qh, 0, GROUP_MM // 2 * (s % 2) + k)

            for s in range(FIRST):
                slot(0, s, False, True)
            with pe.Fori(0, NB - 1) as b:
                for s in range(FIRST, FIRST + SLOTS):
                    slot(b, s, False)
            for s in range(FIRST, SLOTS + 1):
                slot(NB - 1, s, True)

            pe.wait_ge(w_lo_done, FOLDS)
            for qh in range(2):
                for k in range(GROUP_MM):
                    out_step(0, qh, 1, k)

            def out_batch(v, i, first):
                pe.wait_ge(o_ready, v)
                for qh in range(2):
                    for half in range(2):
                        if not first:
                            pe.wait_ge(o_out, v * 4 + (2 * qh + half - 7))
                        for k in range(GROUP_MM):
                            out_step(i, qh, half, k)

            pe.wait_ge(ctx_done, NB * NG)
            out_batch(1, 1, True)
            with pe.Fori(1, NB // 2) as pair:
                for i in range(2):
                    out_batch(pair * 2 + i, i, False)


def kernel(**inputs):
    import numpy as np
    import concourse.bacc as bacc
    from concourse.bass_utils import run_bass_kernel_spmd

    def w(name):
        return np.asarray(inputs["L0_xattn_" + name])

    def by_columns(a):
        a = np.asarray(a).transpose(0, 2, 1).reshape(NB, KT, P, S)
        return a.transpose(0, 2, 1, 3).reshape(NB, P, KT * S)

    def stacked(a):
        t = np.zeros((R, P // R, a.shape[1]), a.dtype)
        t[:, :a.shape[0]] = a
        return t.reshape(P, a.shape[1])

    x = np.asarray(inputs["x"])
    arrays = {
        "xt": by_columns(x),
        "ct": by_columns(inputs["ctx_4096"]),
        "xn": x,
        "wq": w("Wq").reshape(KT, P, D),
        "wkv": np.concatenate([w("Wk"), w("Wv")], axis=1).reshape(KT, P, 2 * KV),
        "wo": w("Wo").reshape(KT, P, D),
        "a4": np.stack([stacked(w(n).T) for n in ("Ak", "Av", "Aq", "Ao")]),
        "b4kv": stacked(np.concatenate([w("Bk"), w("Bv")], axis=1)),
        "b4q": stacked(w("Bq")),
        "b4o": stacked(w("Bo")),
    }
    arrays = {n: np.ascontiguousarray(a) for n, a in arrays.items()}
    nc = bacc.Bacc("TRN2", target_bir_lowering=False, num_devices=1)
    args = [nc.dram_tensor(n, a.shape, mybir.dt.from_np(a.dtype), kind="ExternalInput").ap()
            for n, a in arrays.items()]
    out = nc.dram_tensor("out", (NB, S, D), F32, kind="ExternalOutput").ap()
    xattn(nc, *args, out)
    r = run_bass_kernel_spmd(nc, [arrays], core_ids=[0])
    return r.results[0]["out"]
```

```python
from contextlib import ExitStack

import concourse.bass as bass
from concourse import mybir

P = 128
NB = 8
S = 256
D = 1024
KT = D // P
HD = 32
NG = 8
GH = 4
KV = NG * HD
R = 4
LORA_SCALE = 2.0
SCORE_SCALE = float(HD) ** -0.5
SLOTS = 4 * NG
AHEAD = 4
NORM_AHEAD = 3
FIRST = 3
GROUP_MM = 3 * KT
FILL = 9
DMA = 16

F32 = mybir.dt.float32
F32R = mybir.dt.float32r
ALU = mybir.AluOpType
ACT = mybir.ActivationFunctionType
AXIS = mybir.AxisListType.X

PROLOGUE = [("k", 0, 0), ("k", 1, 0), ("v", 0, 0), ("q", 0, 0), ("q", 1, 0), ("q", 2, 0),
            ("q", 3, 0), ("v", 1, 0)]
PRO_Q = 3
BODY = [("q", 4, 0), ("q", 5, 0), ("k", 0, 1), ("q", 6, 0), ("q", 7, 0), ("k", 1, 1),
        ("q", 0, 1), ("q", 1, 1), ("q", 2, 1), ("q", 3, 1), ("v", 0, 1), ("v", 1, 1)]
LAST = [g for g in BODY if g[2] == 0]
PRO = len(PROLOGUE)
PER = len(BODY)
SPLITS_PER = sum(g[0] != "v" for g in BODY)
SPLITS_PRO = sum(g[0] != "v" for g in PROLOGUE)
assert PER * GROUP_MM == SLOTS * FILL

FOLD_KV, FOLD_Q, FOLD_O = 0, KT, 3 * KT
FOLDS = 5 * KT
WARM_UP = 48
OUT_SLOT = SLOTS - 4
V1_EARLY, V1_SLOT = 16, 4
W_RING = 6


def xattn(nc, xt, ct, xn, wq, wkv, wo, a4, b4kv, b4q, b4o, out):
    with ExitStack() as ctx:
        def sb(name, shape, dt):
            return ctx.enter_context(nc.sbuf_tensor(name, shape, dt))

        def sem(name):
            return ctx.enter_context(nc.semaphore(name))

        w_hl = [sb("w_hi", [P, KT, D], F32R), sb("w_lo", [P, KT, D], F32R)]
        wkv_hl = [sb("wkv_hi", [P, KT, 2 * KV], F32R), sb("wkv_lo", [P, KT, 2 * KV], F32R)]
        x_hl = [sb("x_hi", [P, KT, S], F32R), sb("x_lo", [P, KT, S], F32R)]
        c_hl = [sb("c_hi", [P, KT, S], F32R), sb("c_lo", [P, KT, S], F32R)]
        raw = sb("raw", [P, 4, 2 * S], F32)
        q_stage = sb("q_stage", [P, 2, 2, S], F32R)
        k_stage = sb("k_stage", [P, 2, 2, S], F32R)
        q_stack = sb("q_stack", [P, 2, GH, S], F32R)
        k_stack = sb("k_stack", [P, NG, S], F32R)
        v_sb = sb("v_sb", [P, 2, KV], F32)
        probs = sb("probs", [P, 4, 2, S], F32)
        probs_t = sb("probs_t", [P, 2, 2, GH, S], F32)
        neg_max = sb("neg_max", [P, 4, 2], F32)
        sums = sb("sums", [P, 4, 2], F32)
        rsums = sb("rsums", [P, 4, 2], F32)
        ctx_stage = sb("ctx_stage", [P, 2, S], F32)
        ident = sb("ident", [P, P], F32)
        half_ident = sb("half_ident", [P, P], F32)
        lora = sb("lora", [P, 2, D], F32R)
        w_sum = sb("w_sum", [P, 2, 512], F32)

        probs_flat = probs[:].rearrange("p a b c -> p (a b c)")
        pt_flat = probs_t[:].rearrange("p a b c d -> p (a b c d)")
        lora_kv_a = q_stack[:].rearrange("p a b c -> p (a b c)")
        lora_kv_b = k_stack[:].rearrange("p a b -> p (a b)")
        w_raw = [pt_flat[:, 512 * i:512 * (i + 1)] for i in range(W_RING)]
        w_raw_o = [raw[:, i, :] for i in range(4)]
        b_kv_raw = pt_flat[:, 3072:3584]
        lora_stack = [(probs_flat[:, 0:2 * D], b_kv_raw, lora_kv_a[:, 0:2 * D],
                       lora_kv_b[:, 0:2 * KV], 3)] + [
            (probs_flat[:, 0:D], probs_flat[:, D:2 * D], lora[:, 0, :], lora[:, 1, :], 2)] * 2
        ctx_raw = [pt_flat[:, 2048 * i:2048 * (i + 1)].rearrange("p (g n) -> p g n", g=NG)
                   for i in (1, 0)]
        o_parts = (c_hl, x_hl)
        x_rows = [probs_flat[:, D * i:D * (i + 1)] for i in range(2)]
        out_rows = [raw[:, 2 * i:2 * i + 2, :].rearrange("p a b -> p (a b)") for i in range(2)]

        banks = ctx.enter_context(nc.psum_tensor("banks", [P, 8, 512], F32))
        score_bank = [banks[:, i, :] for i in range(4)]
        turn_bank = [banks[:, 4 + i, :] for i in range(2)]
        proj_bank = [banks[:, 6 + i, :] for i in range(2)]

        q_dram = nc.dram_tensor("q_parts", [4, 2, P, S], F32, kind="Internal").ap()
        k_dram = nc.dram_tensor("k_parts", [2, 2, P, S], F32, kind="Internal").ap()
        ctx_dram = nc.dram_tensor("context", [NB, NG, P, S], F32, kind="Internal").ap()

        raw_in = [sem(f"raw_in{i}") for i in range(4)]
        w_in = [sem(f"w_in{i}") for i in range(W_RING)]
        wo_in = [sem(f"wo_in{i}") for i in range(4)]
        lora_in = [sem(f"lora_in{i}") for i in range(3)]
        q_stored = [sem(f"q_stored{i}") for i in range(2)]
        q_stacked = [sem(f"q_stacked{i}") for i in range(2)]
        k_stored = [sem(f"k_stored{i}") for i in range(2)]
        k_stacked = [sem(f"k_stacked{i}") for i in range(2)]
        ctx_stored = [sem(f"ctx_stored{i}") for i in range(2)]
        ctx_in = [sem(f"ctx_in{i}") for i in range(2)]
        rows_in = [sem(f"rows_in{i}") for i in range(2)]
        out_stored = [sem(f"out_stored{i}") for i in range(2)]
        sp_waits = sem("sp_waits")
        ident_zero = sem("ident_zero")
        ident_ready = sem("ident_ready")
        lora_hi = sem("lora_hi")
        lora_hi_a = sem("lora_hi_a")
        lora_hi_act = sem("lora_hi_act")
        lora_ready = sem("lora_ready")
        lora_b_ready = sem("lora_b_ready")
        fold_mm = sem("fold_mm")
        w_summed = sem("w_summed")
        w_hi_done = sem("w_hi_done")
        w_lo_dve = sem("w_lo_dve")
        w_lo_pool = sem("w_lo_pool")
        c_hi_done = sem("c_hi_done")
        c_ready = sem("c_ready")
        x_hi_done = sem("x_hi_done")
        x_ready = sem("x_ready")
        proj_mm = sem("proj_mm")
        proj_hi = sem("proj_hi")
        proj_out = sem("proj_out")
        scores_mm = sem("scores_mm")
        max_done = sem("max_done")
        exp_done = sem("exp_done")
        turned = sem("turned")
        pt_dve = sem("pt_dve")
        pt_act = sem("pt_act")
        rsum_done = sem("rsum_done")
        norm_done = sem("norm_done")
        ctx_mm = sem("ctx_mm")
        ctx_done = sem("ctx_done")
        o_hi_done = sem("o_hi_done")
        o_ready = sem("o_ready")
        o_mm = sem("o_mm")
        o_out = sem("o_out")

        block = ctx.enter_context(nc.Block())

        def split_number(i, n):
            return n * SPLITS_PER + (SPLITS_PRO + sum(g[0] != "v" for g in BODY[:i]))

        def end_slot(i):
            return FIRST + (GROUP_MM * (i + 1) - 1) // FILL

        def fold_tile(f):
            return divmod(f - FOLD_Q, 2) if f < FOLD_O else ((f - FOLD_O) % KT, (f - FOLD_O) // KT)

        def w_raw_of(f):
            return w_raw[f % W_RING] if f < FOLD_O else w_raw_o[f % 4]

        def stack_ready(engine, n):
            engine.wait_ge(lora_ready, n + 1)
            engine.wait_ge(lora_b_ready, 2 * n + 2)

        def w_landed(f):
            if f < FOLD_O:
                return w_in[f % W_RING], DMA * (f // W_RING + 1)
            return wo_in[f % 4], DMA * ((f - FOLD_O) // 4 + 1)

        def pe_adds(f):
            return f % 2 == 0 if f < FOLD_O else f < FOLD_O + KT

        def sums_to(f):
            return sum(not pe_adds(i) for i in range(f + 1))

        def adds_to(f):
            return sum(pe_adds(i) for i in range(f + 1))

        def sum_of(f):
            return w_sum[:, (sums_to(f) - 1) % 2, :]

        def lows_done(engine, f):
            engine.wait_ge(w_lo_dve, adds_to(f))
            if sums_to(f):
                engine.wait_ge(w_lo_pool, sums_to(f))

        def fold_bank(f):
            return score_bank[f % 4] if f < FOLD_O else proj_bank[f % 2]

        def w_piece(f, part):
            if f < FOLD_Q:
                return wkv_hl[part][:, f, :]
            kt, half = fold_tile(f)
            return w_hl[part][:, kt, 512 * half:512 * (half + 1)]

        def fold_chunks(s):
            early = (16, 17, 19, 20, 21, 23, 24, 25)
            if s in early:
                return [FOLD_O + early.index(s)]
            return [FOLD_O + KT + 2 * (s - OUT_SLOT) + i for i in range(2)] if OUT_SLOT <= s < SLOTS else []

        def turn_of(unit, c):
            return turn_bank[(5 * unit + (0, 2, 3, 4)[c]) % 2]

        def copy_turned(op, unit, c):
            dst = probs_t[:, unit % 2, :, 2 * (c % 2):2 * (c % 2) + 2, P * (c // 2):P * (c // 2 + 1)]
            src = turn_of(unit, c).rearrange("p (t h q) -> p t h q", t=2, h=2)
            return op(dst, src, ACT.Copy) if op == nc.scalar.activation else op(dst, src)

        @block.sync
        def _(sp):
            def wait(semaphore, value):
                sp.wait_ge(semaphore, value)
                if not isinstance(value, int):
                    sp.sem_inc(sp_waits, 1)

            def load_inputs(src, b, j):
                sp.dma_start(raw[:, j, :], src[b, :, 2 * S * j:2 * S * (j + 1)]).then_inc(raw_in[j], DMA)

            def load_w(f):
                if f < FOLD_Q:
                    src = wkv[f]
                else:
                    kt, half = fold_tile(f)
                    src = (wq if f < FOLD_O else wo)[kt, :, 512 * half:512 * (half + 1)]
                before = f - (W_RING if f < FOLD_O else 4)
                if before >= (0 if f < FOLD_O else FOLD_O):
                    if pe_adds(before):
                        wait(fold_mm, before + 1)
                    else:
                        wait(w_summed, sums_to(before))
                sp.dma_start(w_raw_of(f), src).then_inc(w_landed(f)[0], DMA)

            def stack_q(g, fills_of_stage, scores_before):
                wait(q_stored[g % 2], fills_of_stage * DMA)
                if scores_before is not None:
                    wait(scores_mm, scores_before)
                for r, part in enumerate((0, 1, 0)):
                    sp.dma_start(q_stack[HD * r:HD * (r + 1), g % 2].bitcast(F32),
                                 q_dram[g % 4, part].rearrange("(c p) n -> p c n", c=GH)).then_inc(q_stacked[g % 2], DMA)

            def load_ctx(v, i):
                sp.dma_start(ctx_raw[i], ctx_dram[v].rearrange("g p n -> p g n")).then_inc(ctx_in[i], DMA)

            def send_q(g, count):
                wait(proj_out, count)
                sp.dma_start(q_dram[g % 4].rearrange("h p n -> p h n"),
                             q_stage[:, g % 2].bitcast(F32)).then_inc(q_stored[g % 2], DMA)

            def send_k(m, count):
                wait(proj_out, count)
                sp.dma_start(k_dram[m].rearrange("h p n -> p h n"),
                             k_stage[:, m].bitcast(F32)).then_inc(k_stored[m], DMA)

            def stack_k(m, fills, scores_before):
                wait(k_stored[m], fills * DMA)
                if scores_before is not None:
                    wait(scores_mm, scores_before)
                for r, part in enumerate((0, 0, 1)):
                    sp.dma_start(k_stack[HD * r:HD * (r + 1), 4 * m:4 * m + 4].bitcast(F32),
                                 k_dram[m, part].rearrange("(c p) n -> p c n", c=4)).then_inc(k_stacked[m], DMA)

            for i in range(2):
                sp.dma_start(probs_flat[:, D * i:D * (i + 1)], a4[i]).then_inc(lora_in[0], DMA)
            sp.dma_start(b_kv_raw, b4kv).then_inc(lora_in[0], DMA)
            for f in range(4):
                load_w(f)
            for j in range(4):
                load_inputs(ct, 0, j)
            for f in range(4, FOLD_Q):
                load_w(f)
            stack_ready(sp, 0)
            sp.dma_start(probs_flat[:, 0:D], a4[2]).then_inc(lora_in[1], DMA)
            sp.dma_start(probs_flat[:, D:2 * D], b4q).then_inc(lora_in[1], DMA)
            for f in range(FOLD_Q, FOLD_Q + 4):
                load_w(f)
            for j in range(4):
                wait(c_ready, j + 1)
                load_inputs(xt, 0, j)
            for f in range(FOLD_Q + 4, FOLD_Q + W_RING):
                load_w(f)
            for m in range(2):
                send_k(m, m + 1)
            for f in range(FOLD_Q + W_RING, FOLD_O):
                load_w(f)
            stack_ready(sp, 1)
            sp.dma_start(probs_flat[:, 0:D], a4[3]).then_inc(lora_in[2], DMA)
            sp.dma_start(probs_flat[:, D:2 * D], b4o).then_inc(lora_in[2], DMA)
            for m in range(2):
                stack_k(m, 1, None)
            for g in range(4):
                send_q(g, g + PRO_Q + 1)
                if g < 2:
                    stack_q(g, 1, None)
            stack_q(2, 2, 4)
            for i in range(2):
                sp.sem_inc(ctx_stored[i], DMA)

            def body(b, last):
                late_w = iter(range(FOLD_O + 4, FOLDS))
                unit0 = b * NG
                group0 = b * PER + PRO
                score0 = b * SLOTS
                fills = b * 4

                def store_ctx(g):
                    wait(ctx_done, unit0 + (g + 1))
                    sp.dma_start(ctx_dram[b, g], ctx_stage[:, g % 2]).then_inc(ctx_stored[g % 2], DMA)

                def send(i):
                    kind, g, _ = BODY[i] if not last else LAST[i]
                    if kind == "q":
                        send_q(g, group0 + (i + 1))
                    else:
                        send_k(g, group0 + (i + 1))

                pos = {g: i for i, g in enumerate(LAST if last else BODY)}
                for j in range(4):
                    wait(x_ready, b * 4 + (j + 1))
                    if not last:
                        load_inputs(ct, b + 1, j)
                    else:
                        sp.dma_start(raw[:, j, :].rearrange("p (g n) -> p g n", g=2),
                                     ctx_dram[0, 2 * j:2 * j + 2].rearrange("g p n -> p g n")
                                     ).then_inc(raw_in[j], DMA)
                stack_q(3, fills + 2, score0 + 8)
                store_ctx(0)
                send(pos["q", 4, 0])
                stack_q(4, fills + 3, score0 + 12)
                send(pos["q", 5, 0])
                store_ctx(1)
                for j in range(4):
                    wait(c_ready, b * 4 + (j + 5))
                    if not last:
                        load_inputs(xt, b + 1, j)
                    else:
                        load_w(FOLD_O + j)
                stack_q(5, fills + 3, score0 + 16)
                if not last:
                    send(pos["k", 0, 1])
                    stack_k(0, b + 2, score0 + 16)
                store_ctx(2)
                send(pos["q", 6, 0])
                stack_q(6, fills + 4, score0 + 20)
                if last:
                    send(pos["q", 7, 0])
                    for g, loads in ((3, 2), (None, 2), (4, 1), (5, 3), (6, 2), (7, 2)):
                        for _ in range(loads):
                            load_w(next(late_w))
                        if g is None:
                            stack_q(7, fills + 4, score0 + 24)
                        else:
                            store_ctx(g)
                        if g == 6:
                            wait(ctx_mm, NB * NG - 1)
                            for i in range(2):
                                wait(ctx_stored[i], DMA * (1 + 2 * NG // 2))
                            load_ctx(1, 1)
                    return
                store_ctx(3)
                send(pos["q", 7, 0])
                stack_q(7, fills + 4, score0 + 24)
                send(pos["k", 1, 1])
                store_ctx(4)
                send(pos["q", 0, 1])
                stack_q(0, fills + 5, score0 + 28)
                store_ctx(5)
                send(pos["q", 1, 1])
                stack_q(1, fills + 5, score0 + 32)
                stack_k(1, b + 2, score0 + 32)
                send(pos["q", 2, 1])
                store_ctx(6)
                send(pos["q", 3, 1])
                stack_q(2, fills + 6, score0 + 36)
                store_ctx(7)

            with sp.Fori(0, NB - 1) as b:
                body(b, False)
            body(NB - 1, True)

            def load_rows(v, h):
                sp.dma_start(x_rows[h], xn[v, P * h:P * (h + 1), :]).then_inc(rows_in[h], DMA)

            wait(turned, NB * SLOTS)
            for h in range(2):
                load_rows(0, h)
            wait(ctx_mm, NB * NG)
            load_ctx(2, 0)
            for i in range(2):
                wait(ctx_stored[i], DMA * (1 + NB * NG // 2))

            def out_batch(v, i, more_ctx, more_rows):
                if more_ctx:
                    wait(o_ready, v + 1)
                    load_ctx(v + 3, 1 - i)
                for h in range(2):
                    if not more_rows and h == 1:
                        for half in range(2):
                            cols = slice(512 * half, 512 * (half + 1))
                            wait(o_out, v * 4 + (3 + half))
                            sp.dma_start(out[v, P:2 * P, cols], out_rows[h][:, cols]).then_inc(out_stored[h], DMA)
                        continue
                    wait(o_out, v * 4 + (2 * h + 2))
                    sp.dma_start(out[v, P * h:P * (h + 1), :], out_rows[h]).then_inc(out_stored[h], DMA)
                    if more_rows:
                        load_rows(v + 1, h)

            with sp.Fori(0, 2) as pair:
                for i in range(2):
                    out_batch(pair * 2 + i, i, True, True)
            for v in range(4, NB):
                out_batch(v, v % 2, v + 3 < NB, v + 1 < NB)
            for h in range(2):
                wait(out_stored[h], DMA * (NB + 1 + h))

        @block.gpsimd
        def _(pool):
            for i, (tile, value) in enumerate(((ident, 1.0), (half_ident, 0.5))):
                nc.gpsimd.memset(tile[:], 0.0).then_inc(ident_zero, 1)
                pool.wait_ge(ident_zero, i + 1)
                nc.gpsimd.affine_select(out=tile[:], in_=tile[:], compare_op=ALU.not_equal, fill=value,
                                        base=0, pattern=[[-1, P]],
                                        channel_multiplier=1).then_inc(ident_ready, 1)

            def c_low(j, count):
                cols = [t[:, 2 * j:2 * j + 2, :].rearrange("p a b -> p (a b)") for t in c_hl]
                pool.wait_ge(c_hi_done, count)
                nc.gpsimd.tensor_tensor(cols[1], raw[:, j, :], cols[0], ALU.subtract).then_inc(c_ready, 1)

            def w_low(f):
                pool.wait_ge(w_hi_done, f + 1)
                nc.gpsimd.tensor_tensor(w_piece(f, 1), sum_of(f), w_piece(f, 0),
                                        ALU.subtract).then_inc(w_lo_pool, 1)

            def stack_b_lows(n, before, count):
                pool.wait_ge(lora_hi, n + 1)
                pool.wait_ge(before, count)
                _, b_raw, _, b_dst, _ = lora_stack[n]
                for i, rows in enumerate((slice(32, 64), slice(96, 128))):
                    nc.gpsimd.tensor_tensor(b_dst[rows], b_raw[rows], b_dst[rows],
                                            ALU.subtract).then_inc(lora_b_ready, 1)
                    pool.wait_ge(lora_b_ready, 2 * n + i + 1)

            stack_b_lows(0, ident_ready, 2)
            for f in range(1, FOLD_Q, 2):
                w_low(f)
            stack_b_lows(1, w_lo_pool, sums_to(FOLD_Q - 1))
            for f in range(FOLD_Q + 1, FOLD_O, 2):
                w_low(f)
            stack_b_lows(2, w_lo_pool, sums_to(FOLD_O - 1))

            def normalize(m, c):
                pool.wait_ge(rsum_done, m + 1)
                nc.gpsimd.tensor_tensor(probs[:, c], probs[:, c],
                                        rsums[:, c, :].unsqueeze(2).broadcast_to([P, 2, S]),
                                        ALU.mult).then_inc(norm_done, 1)

            def slot(b, s, last):
                if 5 <= s < 9:
                    j = s - 5
                    c_low(j, b * 4 + (j + 5))
                if not (last and s + NORM_AHEAD >= SLOTS):
                    normalize(b * SLOTS + (s + NORM_AHEAD), (s + NORM_AHEAD) % 4)
                if last:
                    for f in fold_chunks(s):
                        if not pe_adds(f):
                            w_low(f)

            for m in range(FIRST + NORM_AHEAD):
                normalize(m, m % 4)
            with pool.Fori(0, NB - 1) as b:
                for s in range(FIRST, FIRST + SLOTS):
                    slot(b, s, False)
            for s in range(FIRST, SLOTS):
                slot(NB - 1, s, True)

        @block.scalar
        def _(act):
            def high(parts, j, done, fills):
                act.wait_ge(raw_in[j], fills * DMA)
                nc.scalar.activation(parts[0][:, 2 * j:2 * j + 2, :].rearrange("p a b -> p (a b)"),
                                     raw[:, j, :], ACT.Copy).then_inc(done, 1)

            def w_high(f):
                if pe_adds(f):
                    act.wait_ge(fold_mm, f + 1)
                    nc.scalar.activation(w_piece(f, 0), fold_bank(f), ACT.Copy,
                                         scale=LORA_SCALE).then_inc(w_hi_done, 1)
                else:
                    act.wait_ge(w_summed, sums_to(f))
                    nc.scalar.activation(w_piece(f, 0), sum_of(f), ACT.Copy).then_inc(w_hi_done, 1)

            def proj_high(kind, i, bank, group_id, stored):
                act.wait_ge(proj_mm, group_id + 1)
                if kind == "q":
                    if stored is not None:
                        act.wait_ge(q_stored[i % 2], stored)
                    nc.scalar.activation(q_stage[:, i % 2, 0, :], proj_bank[bank][:, 0:S],
                                         ACT.Copy).then_inc(proj_hi, 1)
                else:
                    if stored is not None:
                        act.wait_ge(k_stored[i], stored)
                    nc.scalar.activation(k_stage[:, i, 0, :], proj_bank[bank][:, 0:S],
                                         ACT.Copy, scale=-SCORE_SCALE).then_inc(proj_hi, 1)

            def exps(m, c):
                act.wait_ge(max_done, m + 1)
                for h in range(2):
                    last = nc.scalar.activation(
                        probs[:, c, h, :], score_bank[c][:, S * h:S * (h + 1)], ACT.Exp,
                        bias=neg_max[:, c, h:h + 1], scale=-1.0, accum_out=sums[:, c, h:h + 1])
                last.then_inc(exp_done, 1)

            def build_stack(n):
                a_raw, _, a_dst, _, loads = lora_stack[n]
                half = a_raw.shape[1] // 2
                act.wait_ge(lora_in[n], DMA * loads)
                if n == 2:
                    act.wait_ge(fold_mm, FOLD_O)
                nc.scalar.activation(a_dst[:, half:], a_raw[:, half:], ACT.Copy).then_inc(lora_hi_act, 1)

            build_stack(0)
            for j in range(2):
                high(c_hl, j, c_hi_done, 1)
            for f in range(FOLD_O):
                if f == FOLD_Q:
                    build_stack(1)
                    for m in range(2):
                        proj_high("k", m, m, m, None)
                    for j in range(4):
                        high(x_hl, j, x_hi_done, 2)
                w_high(f)
                if f < 2:
                    high(c_hl, 2 + f, c_hi_done, 1)
            for g in range(4):
                if g == 2:
                    build_stack(2)
                proj_high("q", g, (g + PRO_Q) % 2, g + PRO_Q, DMA if g >= 2 else None)
            stack_ready(act, 2)
            for m in range(4):
                exps(m, m)

            def slot(b, s, last, prologue=False):
                n = b * SLOTS
                unit = s // 4
                c = s % 4
                if c == 3:
                    act.wait_ge(turned, n + (s + 1))
                    copy_turned(nc.scalar.activation, unit, c).then_inc(pt_act, 1)
                groups = [] if prologue else (LAST if last else BODY)
                for i, (kind, gi, nxt) in enumerate(groups):
                    if end_slot(i) + 1 == s and kind != "v":
                        fills = b * 4 + (4 * nxt + gi // 2) if kind == "q" else b + 1
                        proj_high(kind, gi, i % 2, b * PER + (PRO + i), fills * DMA)
                if not (last and s + AHEAD >= SLOTS):
                    act.wait_ge(turned, n + (s + 1))
                    exps(n + (s + AHEAD), c)
                if last:
                    for f in fold_chunks(s):
                        w_high(f)
                if not prologue and s in (4, 5):
                    for j in (2 * (s - 4), 2 * (s - 4) + 1):
                        act.wait_ge(proj_mm, b * PER + PRO)
                        high(c_hl, j, c_hi_done, b * 2 + 3)
                if not prologue and not last and s in (16, 17):
                    for j in (2 * (s - 16), 2 * (s - 16) + 1):
                        act.wait_ge(proj_mm, b * PER + (PRO + BODY.index(("q", 7, 0)) + 1))
                        high(x_hl, j, x_hi_done, b * 2 + 4)

            for s in range(FIRST):
                slot(0, s, False, True)
            with act.Fori(0, NB - 1) as b:
                for s in range(FIRST, FIRST + SLOTS):
                    slot(b, s, False)
            for s in range(FIRST, SLOTS + 2):
                slot(NB - 1, s, True)

            def o_high(i, fills):
                act.wait_ge(ctx_in[i], fills * DMA)
                nc.scalar.activation(o_parts[i][0][:], ctx_raw[i], ACT.Copy).then_inc(o_hi_done, 1)

            o_high(1, 1)
            with act.Fori(1, NB // 2) as pair:
                for i in range(2):
                    act.wait_ge(o_mm, pair * 8 + (4 * i - 4))
                    o_high(i, pair + i)

        @block.vector
        def _(dve):
            def build_stack(n):
                a_raw, b_raw, a_dst, b_dst, loads = lora_stack[n]
                half = a_raw.shape[1] // 2
                dve.wait_ge(lora_in[n], DMA * loads)
                if n == 2:
                    dve.wait_ge(fold_mm, FOLD_O)
                nc.vector.tensor_copy(b_dst, b_raw).then_inc(lora_hi, 1)
                nc.vector.tensor_copy(a_dst[:, 0:half], a_raw[:, 0:half]).then_inc(lora_hi_a, 1)
                dve.wait_ge(lora_hi_a, n + 1)
                dve.wait_ge(lora_hi_act, n + 1)
                nc.vector.tensor_tensor(a_dst[64:128], a_raw[64:128], a_dst[64:128],
                                        ALU.subtract).then_inc(lora_ready, 1)

            def w_total(f):
                dve.wait_ge(fold_mm, f + 1)
                dve.wait_ge(*w_landed(f))
                if sums_to(f) > 2:
                    dve.wait_ge(w_lo_pool, sums_to(f) - 2)
                nc.vector.scalar_tensor_tensor(
                    out=sum_of(f), in0=fold_bank(f), scalar=LORA_SCALE, in1=w_raw_of(f),
                    op0=ALU.mult, op1=ALU.add).then_inc(w_summed, 1)

            def w_low(f):
                dve.wait_ge(w_hi_done, f + 1)
                nc.vector.scalar_tensor_tensor(
                    out=w_piece(f, 1), in0=fold_bank(f), scalar=LORA_SCALE, in1=w_piece(f, 0),
                    op0=ALU.mult, op1=ALU.subtract).then_inc(w_lo_dve, 1)

            def proj_low(kind, i, bank, group_id, splits, ctxs):
                src = proj_bank[bank][:, 0:S]
                if kind == "v":
                    dve.wait_ge(proj_mm, group_id + 1)
                    if ctxs is not None:
                        dve.wait_ge(ctx_mm, ctxs)
                    nc.vector.tensor_copy(v_sb[:, i, :], src).then_inc(proj_out, 1)
                elif kind == "k":
                    dve.wait_ge(proj_hi, splits)
                    nc.vector.scalar_tensor_tensor(
                        out=k_stage[:, i, 1, :], in0=src, scalar=-SCORE_SCALE, in1=k_stage[:, i, 0, :],
                        op0=ALU.mult, op1=ALU.subtract).then_inc(proj_out, 1)
                else:
                    dve.wait_ge(proj_hi, splits)
                    nc.vector.tensor_tensor(q_stage[:, i % 2, 1, :], src, q_stage[:, i % 2, 0, :],
                                            ALU.subtract).then_inc(proj_out, 1)

            def row_max(m, c):
                dve.wait_ge(scores_mm, m + 1)
                nc.vector.tensor_reduce(out=neg_max[:, c, :],
                                        in_=score_bank[c].rearrange("p (h t) -> p h t", h=2),
                                        axis=AXIS, op=ALU.min).then_inc(max_done, 1)

            def input_low(parts, j, hi_done, ready, count):
                cols = [t[:, 2 * j:2 * j + 2, :].rearrange("p a b -> p (a b)") for t in parts]
                dve.wait_ge(hi_done, count)
                nc.vector.tensor_tensor(cols[1], raw[:, j, :], cols[0], ALU.subtract).then_inc(ready, 1)

            build_stack(0)
            for f in range(0, FOLD_O, 2):
                if f == FOLD_Q:
                    build_stack(1)
                    for m in range(2):
                        proj_low("k", m, m, m, m + 1, None)
                    for j in range(4):
                        input_low(x_hl, j, x_hi_done, x_ready, j + 1)
                if f == 0:
                    for j in range(2):
                        input_low(c_hl, j, c_hi_done, c_ready, j + 1)
                w_total(f + 1)
                w_low(f)
                if f < 4:
                    input_low(c_hl, 2 + f // 2, c_hi_done, c_ready, 3 + f // 2)
                if f == FOLD_Q:
                    proj_low("v", 0, 0, PRO_Q - 1, None, None)
            for g in range(4):
                if g == 2:
                    build_stack(2)
                proj_low("q", g, (g + PRO_Q) % 2, g + PRO_Q, 3 + g, None)
            def reciprocal(m, c):
                dve.wait_ge(exp_done, m + 1)
                nc.vector.reciprocal(rsums[:, c, :], sums[:, c, :]).then_inc(rsum_done, 1)

            for m in range(4):
                row_max(m, m)
            for m in range(NORM_AHEAD):
                reciprocal(m, m)

            def slot(b, s, last, prologue=False):
                n = b * SLOTS
                unit, c = s // 4, s % 4
                if c == 1 and not prologue:
                    u = unit - 1
                    dve.wait_ge(ctx_mm, b * NG + (u + 1))
                    dve.wait_ge(ctx_stored[u % 2], b * (4 * DMA) + DMA * (u // 2 + 1))
                    nc.vector.tensor_copy(ctx_stage[:, u % 2, :],
                                          turn_bank[(5 * unit + 1) % 2][:, 0:S]).then_inc(ctx_done, 1)
                if c != 3 and not (last and s >= SLOTS):
                    dve.wait_ge(turned, n + (s + 1))
                    copy_turned(nc.vector.tensor_copy, unit, c).then_inc(pt_dve, 1)
                if not (last and s + AHEAD >= SLOTS):
                    row_max(n + (s + AHEAD), c)
                if s in (17, 18, 19, 20) and not last:
                    input_low(x_hl, s - 17, x_hi_done, x_ready, b * 4 + (s - 17 + 5))
                if not (last and s + NORM_AHEAD >= SLOTS):
                    reciprocal(n + (s + NORM_AHEAD), (s + NORM_AHEAD) % 4)
                if prologue:
                    return
                if s == FIRST:
                    proj_low("v", 1, 1, b * PER + (PRO - 1), None, None)
                if last:
                    for f in fold_chunks(s - 1):
                        if pe_adds(f):
                            w_low(f)
                    for f in fold_chunks(s):
                        if not pe_adds(f):
                            w_total(f)
                for i, (kind, gi, nxt) in enumerate(LAST if last else BODY):
                    if end_slot(i) + 1 == s:
                        proj_low(kind, gi, i % 2, b * PER + (PRO + i),
                                 split_number(i + 1, b) if kind != "v" and not last else
                                 b * SPLITS_PER + (SPLITS_PRO + i + 1),
                                 b * NG + NG)

            for s in range(FIRST):
                slot(0, s, False, True)
            with dve.Fori(0, NB - 1) as b:
                for s in range(FIRST, FIRST + SLOTS):
                    slot(b, s, False)
            for s in range(FIRST, SLOTS + 2):
                slot(NB - 1, s, True)

            for h in range(2):
                dve.sem_inc(out_stored[h], DMA)

            def o_low(i, count):
                dve.wait_ge(o_hi_done, count)
                nc.vector.tensor_tensor(o_parts[i][1][:], ctx_raw[i], o_parts[i][0][:],
                                        ALU.subtract).then_inc(o_ready, 1)

            def rows_out(v, i):
                for h in range(2):
                    dve.wait_ge(rows_in[h], v * DMA + DMA)
                    dve.wait_ge(out_stored[h], v * DMA + DMA)
                    for half in range(2):
                        dve.wait_ge(o_mm, v * 4 + ((1, 3), (3, 4))[h][half])
                        cols = slice(512 * half, 512 * (half + 1))
                        nc.vector.tensor_tensor(out_rows[h][:, cols], banks[:, 4 * i + 2 * h + half, :],
                                                x_rows[h][:, cols], ALU.add).then_inc(o_out, 1)

            with dve.Fori(0, NB // 2 - 1) as pair:
                for i in range(2):
                    o_low(1 - i, pair * 2 + (i + 1))
                    rows_out(pair * 2 + i, i)
            o_low(1, NB - 1)
            rows_out(NB - 2, 0)
            rows_out(NB - 1, 1)

        @block.tensor
        def _(pe):
            def fold_mms(f):
                before = f - (4 if f < FOLD_O else 2)
                if before >= (0 if f < FOLD_O else FOLD_O):
                    if pe_adds(before):
                        pe.wait_ge(w_lo_dve, adds_to(before))
                    else:
                        pe.wait_ge(w_summed, sums_to(before))
                bank = fold_bank(f)
                if pe_adds(f):
                    pe.wait_ge(*w_landed(f))
                if f < FOLD_Q:
                    pieces = [(slice(KV * i, KV * (i + 1)), lora_kv_a[:, D * i + P * f:D * i + P * (f + 1)],
                               lora_kv_b[:, KV * i:KV * (i + 1)]) for i in range(2)]
                else:
                    kt, half = fold_tile(f)
                    pieces = [(slice(0, 512), lora[:, 0, P * kt:P * (kt + 1)],
                               lora[:, 1, 512 * half:512 * (half + 1)])]
                for cols, a, b in pieces:
                    if pe_adds(f):
                        nc.tensor.matmul(bank[:, cols], half_ident[:], w_raw_of(f)[:, cols],
                                         start=True, stop=False)
                    last = nc.tensor.matmul(bank[:, cols], a, b, start=not pe_adds(f), stop=True)
                last.then_inc(fold_mm, 1)

            def group_step(kind, i, bank, k):
                kt, product = divmod(k, 3)
                w_part, t_part = ((0, 0), (0, 1), (1, 0))[product]
                if kind == "q":
                    lhs, rhs = w_hl[w_part][:, kt, P * i:P * (i + 1)], x_hl[t_part][:, kt, :]
                elif kind == "k":
                    lhs, rhs = wkv_hl[w_part][:, kt, P * i:P * (i + 1)], c_hl[t_part][:, kt, :]
                else:
                    lhs, rhs = c_hl[t_part][:, kt, P * i:P * (i + 1)], wkv_hl[w_part][:, kt, KV:2 * KV]
                mm = nc.tensor.matmul(proj_bank[bank][:, 0:S], lhs, rhs, start=(k == 0),
                                      stop=(k == GROUP_MM - 1))
                if k == GROUP_MM - 1:
                    mm.then_inc(proj_mm, 1)

            def inputs_ready(kind, i, k, batches):
                if i == 0 and kind in "qk" and k % 6 == 0:
                    pe.wait_ge(x_ready if kind == "q" else c_ready, batches * 4 + (k // 6 + 1))

            def scores(m, g, c):
                qh, hp = c // 2, c % 2
                for h in range(2):
                    head = 2 * hp + h
                    last = nc.tensor.matmul(
                        score_bank[c][:, S * h:S * (h + 1)],
                        q_stack[0:3 * HD, g % 2, head, P * qh:P * (qh + 1)],
                        k_stack[0:3 * HD, g, :], start=True, stop=True)
                last.then_inc(scores_mm, 1)

            def stacks_ready(b, g):
                pe.wait_ge(q_stacked[g % 2], b * (12 * DMA) + 3 * DMA * (g // 2 + 1))
                if g % 4 == 0:
                    pe.wait_ge(k_stacked[g // 4], b * (3 * DMA) + 3 * DMA)

            def turn(unit, c):
                bank = turn_of(unit, c)
                for t in range(2):
                    for h in range(2):
                        last = nc.tensor.transpose(bank[:, P * (2 * t + h):P * (2 * t + h + 1)],
                                                   probs[:, c, h, P * t:P * (t + 1)], ident[:])
                last.then_inc(turned, 1)

            def context(unit):
                bank = turn_bank[(5 * unit + 6) % 2]
                for t in range(2):
                    for h in range(GH):
                        last = nc.tensor.matmul(
                            bank[HD * h:HD * (h + 1), 0:S],
                            v_sb[:, t, HD * (unit % NG):HD * (unit % NG + 1)],
                            probs_t[:, unit % 2, t, h, :], start=(t == 0), stop=(t == 1),
                            tile_position=(0, HD * h))
                last.then_inc(ctx_mm, 1)

            def out_step(i, qh, half, k):
                kt, product = divmod(k, 3)
                w_part, t_part = ((0, 0), (0, 1), (1, 0))[product]
                mm = nc.tensor.matmul(
                    banks[:, 4 * i + 2 * qh + half, :], o_parts[i][t_part][:, kt, P * qh:P * (qh + 1)],
                    w_hl[w_part][:, kt, 512 * half:512 * (half + 1)],
                    start=(k == 0), stop=(k == GROUP_MM - 1))
                if k == GROUP_MM - 1:
                    mm.then_inc(o_mm, 1)

            pe.wait_ge(ident_ready, 1)
            with pe.Fori(0, WARM_UP // 8) as _:
                for _ in range(8):
                    nc.tensor.transpose(proj_bank[0][:, 0:P], ident[:], ident[:])
            pe.wait_ge(ident_ready, 2)
            stack_ready(pe, 0)
            for f in range(FOLD_Q):
                fold_mms(f)
            for j, (kind, i, _) in enumerate(PROLOGUE):
                if j == PRO_Q:
                    stack_ready(pe, 1)
                    for f in range(FOLD_Q, FOLD_O):
                        fold_mms(f)
                if j == PRO - 1:
                    stacks_ready(0, 0)
                    for m in range(4):
                        scores(m, 0, m)
                if j >= 2:
                    pe.wait_ge(proj_out, j - 1)
                for k in range(GROUP_MM if j < PRO - 1 else V1_EARLY):
                    inputs_ready(kind, i, k, 0)
                    if j == 0 and k % 3 == 0:
                        lows_done(pe, k // 3)
                    if j == PRO_Q and k % 3 == 0:
                        lows_done(pe, FOLD_Q + 2 * (k // 3) + 1)
                    group_step(kind, i, j % 2, k)

            def slot(b, s, last, prologue=False):
                n = b * SLOTS
                unit, c = s // 4, s % 4
                if s < SLOTS or not last:
                    pe.wait_ge(norm_done, n + (s + 1))
                    if c == 0 and not prologue:
                        pe.wait_ge(pt_dve, b * (3 * NG) + 3 * unit)
                    if c in (1, 3):
                        pe.wait_ge(pt_dve, b * (3 * NG) + (3 * unit + (c + 1) // 2))
                    if c == 2 and not prologue:
                        pe.wait_ge(ctx_done, b * NG + unit)
                    turn(unit, c)
                if not (last and s + AHEAD >= SLOTS):
                    nxt = (s + AHEAD) // 4
                    if c == 0:
                        if nxt < NG:
                            stacks_ready(b, nxt)
                        else:
                            stacks_ready(b + 1, nxt % NG)
                    scores(n + (s + AHEAD), nxt % NG, c)
                if prologue:
                    done = V1_EARLY + V1_SLOT * s
                    for k in range(done, min(done + V1_SLOT, GROUP_MM)):
                        group_step("v", 1, (PRO - 1) % 2, k)
                    return
                groups = LAST if last else BODY
                for k in range(FILL * (s - FIRST), FILL * (s - FIRST + 1)):
                    j, step = divmod(k, GROUP_MM)
                    if j >= len(groups):
                        break
                    kind, i, nx = groups[j]
                    if step == 0:
                        pe.wait_ge(proj_out, b * PER + (PRO + j - 1))
                    if nx:
                        inputs_ready(kind, i, step, b + 1)
                    group_step(kind, i, j % 2, step)
                if last:
                    chunks = fold_chunks(s)
                    if s < OUT_SLOT:
                        for f in chunks:
                            if f == FOLD_O:
                                pe.wait_ge(proj_out, b * PER + (PRO + len(LAST)))
                            fold_mms(f)
                    elif s < SLOTS:
                        qh = (s - OUT_SLOT) // 2
                        if s == OUT_SLOT:
                            pe.wait_ge(c_ready, 4 * NB + 4)
                            lows_done(pe, FOLD_O + KT - 1)
                        if s == OUT_SLOT + 2:
                            pe.wait_ge(exp_done, n + (SLOTS - 1))
                        for k in range(GROUP_MM // 2):
                            if k % 6 == 0:
                                fold_mms(chunks[k // 6])
                            out_step(0, qh, 0, GROUP_MM // 2 * (s % 2) + k)
                if c == 0:
                    u = unit - 1
                    pe.wait_ge(pt_act, b * NG + (u + 1))
                    pe.wait_ge(pt_dve, b * (3 * NG) + 3 * (u + 1))
                    if u == 0:
                        pe.wait_ge(proj_out, b * PER + PRO)
                    context(u)

            for s in range(FIRST):
                slot(0, s, False, True)
            with pe.Fori(0, NB - 1) as b:
                for s in range(FIRST, FIRST + SLOTS):
                    slot(b, s, False)
            for s in range(FIRST, SLOTS + 1):
                slot(NB - 1, s, True)

            lows_done(pe, FOLDS - 1)
            for qh in range(2):
                for k in range(GROUP_MM):
                    out_step(0, qh, 1, k)

            def out_batch(v, i, first):
                pe.wait_ge(o_ready, v)
                for qh in range(2):
                    for half in range(2):
                        if not first:
                            pe.wait_ge(o_out, v * 4 + (2 * qh + half - 7))
                        for k in range(GROUP_MM):
                            out_step(i, qh, half, k)

            pe.wait_ge(ctx_done, NB * NG)
            out_batch(1, 1, True)
            with pe.Fori(1, NB // 2) as pair:
                for i in range(2):
                    out_batch(pair * 2 + i, i, False)


def kernel(**inputs):
    import numpy as np
    import concourse.bacc as bacc
    from concourse.bass_utils import run_bass_kernel_spmd

    def w(name):
        return np.asarray(inputs["L0_xattn_" + name])

    def by_columns(a):
        a = np.asarray(a).transpose(0, 2, 1).reshape(NB, KT, P, S)
        return a.transpose(0, 2, 1, 3).reshape(NB, P, KT * S)

    def stacked(a):
        t = np.zeros((R, P // R, a.shape[1]), a.dtype)
        t[:, :a.shape[0]] = a
        return t.reshape(P, a.shape[1])

    x = np.asarray(inputs["x"])
    arrays = {
        "xt": by_columns(x),
        "ct": by_columns(inputs["ctx_4096"]),
        "xn": x,
        "wq": w("Wq").reshape(KT, P, D),
        "wkv": np.concatenate([w("Wk"), w("Wv")], axis=1).reshape(KT, P, 2 * KV),
        "wo": w("Wo").reshape(KT, P, D),
        "a4": np.stack([stacked(w(n).T) for n in ("Ak", "Av", "Aq", "Ao")]),
        "b4kv": stacked(np.concatenate([w("Bk"), w("Bv")], axis=1)),
        "b4q": stacked(w("Bq")),
        "b4o": stacked(w("Bo")),
    }
    arrays = {n: np.ascontiguousarray(a) for n, a in arrays.items()}
    nc = bacc.Bacc("TRN2", target_bir_lowering=False, num_devices=1)
    args = [nc.dram_tensor(n, a.shape, mybir.dt.from_np(a.dtype), kind="ExternalInput").ap()
            for n, a in arrays.items()]
    out = nc.dram_tensor("out", (NB, S, D), F32, kind="ExternalOutput").ap()
    xattn(nc, *args, out)
    r = run_bass_kernel_spmd(nc, [arrays], core_ids=[0])
    return r.results[0]["out"]
```
